# Optimizing a Trainium2 kernel written in Bass

```python
import numpy as np
import jax
import jax.numpy as jnp

def _softmax(x, axis=-1):
    return jax.nn.softmax(x, axis=axis)

def _gelu(x):
    return jax.nn.gelu(x, approximate=True)

def _silu(x):
    return jax.nn.silu(x)

def _sigmoid(x):
    return jax.nn.sigmoid(x)

def _layernorm(x, axis=-1, eps=1e-05):
    m = jnp.mean(x, axis=axis, keepdims=True)
    v = jnp.var(x, axis=axis, keepdims=True)
    return (x - m) / jnp.sqrt(v + eps)

def _scatter_add(tgt, idx, src, axis=0):
    return tgt.at[idx].add(src)

def _segment_sum(src, seg, n):
    return jax.ops.segment_sum(src, seg, n)
kernel_name = 'mk_dlrm_tower_d1_rec_r8_e823e0'

def setup_inputs(seed: int=0):
    np.random.seed(seed)
    _w = jnp.asarray

    def _rec_inputs():
        import jax
        import jax.numpy as jnp
        _tk = jax.random.key(seed)
        ids = jnp.stack([jax.random.randint(jax.random.fold_in(_tk, 200 + f), (512,), 0, v, jnp.int32) for f, v in enumerate([12500, 1250, 125000, 1000, 12500, 1250, 1250, 1000, 12500, 1000, 1250, 12500, 1250, 1250, 1000, 1000, 1250, 12500, 1250, 1250, 12500, 12500, 1000, 1000, 1250, 1250])], axis=1)
        tbl_0 = 0.05 * jax.random.normal(jax.random.fold_in(_tk, 500 + 0), (12500, 128), jnp.float32)
        tbl_1 = 0.05 * jax.random.normal(jax.random.fold_in(_tk, 500 + 1), (1250, 128), jnp.float32)
        tbl_2 = 0.05 * jax.random.normal(jax.random.fold_in(_tk, 500 + 2), (125000, 128), jnp.float32)
        tbl_3 = 0.05 * jax.random.normal(jax.random.fold_in(_tk, 500 + 3), (1000, 128), jnp.float32)
        tbl_4 = 0.05 * jax.random.normal(jax.random.fold_in(_tk, 500 + 4), (12500, 128), jnp.float32)
        tbl_5 = 0.05 * jax.random.normal(jax.random.fold_in(_tk, 500 + 5), (1250, 128), jnp.float32)
        tbl_6 = 0.05 * jax.random.normal(jax.random.fold_in(_tk, 500 + 6), (1250, 128), jnp.float32)
        tbl_7 = 0.05 * jax.random.normal(jax.random.fold_in(_tk, 500 + 7), (1000, 128), jnp.float32)
        tbl_8 = 0.05 * jax.random.normal(jax.random.fold_in(_tk, 500 + 8), (12500, 128), jnp.float32)
        tbl_9 = 0.05 * jax.random.normal(jax.random.fold_in(_tk, 500 + 9), (1000, 128), jnp.float32)
        tbl_10 = 0.05 * jax.random.normal(jax.random.fold_in(_tk, 500 + 10), (1250, 128), jnp.float32)
        tbl_11 = 0.05 * jax.random.normal(jax.random.fold_in(_tk, 500 + 11), (12500, 128), jnp.float32)
        tbl_12 = 0.05 * jax.random.normal(jax.random.fold_in(_tk, 500 + 12), (1250, 128), jnp.float32)
        tbl_13 = 0.05 * jax.random.normal(jax.random.fold_in(_tk, 500 + 13), (1250, 128), jnp.float32)
        tbl_14 = 0.05 * jax.random.normal(jax.random.fold_in(_tk, 500 + 14), (1000, 128), jnp.float32)
        tbl_15 = 0.05 * jax.random.normal(jax.random.fold_in(_tk, 500 + 15), (1000, 128), jnp.float32)
        tbl_16 = 0.05 * jax.random.normal(jax.random.fold_in(_tk, 500 + 16), (1250, 128), jnp.float32)
        tbl_17 = 0.05 * jax.random.normal(jax.random.fold_in(_tk, 500 + 17), (12500, 128), jnp.float32)
        tbl_18 = 0.05 * jax.random.normal(jax.random.fold_in(_tk, 500 + 18), (1250, 128), jnp.float32)
        tbl_19 = 0.05 * jax.random.normal(jax.random.fold_in(_tk, 500 + 19), (1250, 128), jnp.float32)
        tbl_20 = 0.05 * jax.random.normal(jax.random.fold_in(_tk, 500 + 20), (12500, 128), jnp.float32)
        tbl_21 = 0.05 * jax.random.normal(jax.random.fold_in(_tk, 500 + 21), (12500, 128), jnp.float32)
        tbl_22 = 0.05 * jax.random.normal(jax.random.fold_in(_tk, 500 + 22), (1000, 128), jnp.float32)
        tbl_23 = 0.05 * jax.random.normal(jax.random.fold_in(_tk, 500 + 23), (1000, 128), jnp.float32)
        tbl_24 = 0.05 * jax.random.normal(jax.random.fold_in(_tk, 500 + 24), (1250, 128), jnp.float32)
        tbl_25 = 0.05 * jax.random.normal(jax.random.fold_in(_tk, 500 + 25), (1250, 128), jnp.float32)
        _rk = jax.random.fold_in(_tk, 7)
        r_dense_features = -0.000520686 + 1.00062 * jax.random.normal(jax.random.fold_in(_rk, 101), (512, 128), jnp.float32)
        W_top1 = 0.0405887 * jax.random.normal(jax.random.fold_in(_tk, 801), (607, 512), jnp.float32)
        W_top2 = 0.0441942 * jax.random.normal(jax.random.fold_in(_tk, 802), (512, 256), jnp.float32)
        W_top3 = 0.0625 * jax.random.normal(jax.random.fold_in(_tk, 803), (256, 1), jnp.float32)
        b_top1 = jnp.zeros((512,), jnp.float32)
        b_top2 = jnp.zeros((256,), jnp.float32)
        return (r_dense_features, ids, tbl_0, tbl_1, tbl_2, tbl_3, tbl_4, tbl_5, tbl_6, tbl_7, tbl_8, tbl_9, tbl_10, tbl_11, tbl_12, tbl_13, tbl_14, tbl_15, tbl_16, tbl_17, tbl_18, tbl_19, tbl_20, tbl_21, tbl_22, tbl_23, tbl_24, tbl_25, W_top1, b_top1, W_top2, b_top2, W_top3)
    r_dense_features, ids, tbl_0, tbl_1, tbl_2, tbl_3, tbl_4, tbl_5, tbl_6, tbl_7, tbl_8, tbl_9, tbl_10, tbl_11, tbl_12, tbl_13, tbl_14, tbl_15, tbl_16, tbl_17, tbl_18, tbl_19, tbl_20, tbl_21, tbl_22, tbl_23, tbl_24, tbl_25, W_top1, b_top1, W_top2, b_top2, W_top3 = _rec_inputs()

    def _L0_rec_setup():
        import jax, jax.numpy as jnp
        import numpy as np
        B, F, D = (2048, 26, 128)
        key = jax.random.key(seed)
        k1, k2 = jax.random.split(key)
        dense_features = jax.random.normal(k1, (B, D), dtype=jnp.float32)
        sparse_values = jax.random.normal(k2, (B, F, D), dtype=jnp.float32)
        return {'dense_features': dense_features, 'sparse_values': sparse_values}
    _L0_rec_all = _L0_rec_setup()
    _L0_rec_in = {k: v for k, v in _L0_rec_all.items() if k in ()}
    del _L0_rec_all
    return {'r_dense_features': r_dense_features, 'ids': ids, 'tbl_0': tbl_0, 'tbl_1': tbl_1, 'tbl_2': tbl_2, 'tbl_3': tbl_3, 'tbl_4': tbl_4, 'tbl_5': tbl_5, 'tbl_6': tbl_6, 'tbl_7': tbl_7, 'tbl_8': tbl_8, 'tbl_9': tbl_9, 'tbl_10': tbl_10, 'tbl_11': tbl_11, 'tbl_12': tbl_12, 'tbl_13': tbl_13, 'tbl_14': tbl_14, 'tbl_15': tbl_15, 'tbl_16': tbl_16, 'tbl_17': tbl_17, 'tbl_18': tbl_18, 'tbl_19': tbl_19, 'tbl_20': tbl_20, 'tbl_21': tbl_21, 'tbl_22': tbl_22, 'tbl_23': tbl_23, 'tbl_24': tbl_24, 'tbl_25': tbl_25, 'W_top1': W_top1, 'b_top1': b_top1, 'W_top2': W_top2, 'b_top2': b_top2, 'W_top3': W_top3}

def reference(r_dense_features, ids, tbl_0, tbl_1, tbl_2, tbl_3, tbl_4, tbl_5, tbl_6, tbl_7, tbl_8, tbl_9, tbl_10, tbl_11, tbl_12, tbl_13, tbl_14, tbl_15, tbl_16, tbl_17, tbl_18, tbl_19, tbl_20, tbl_21, tbl_22, tbl_23, tbl_24, tbl_25, W_top1, b_top1, W_top2, b_top2, W_top3):
    import jax
    import jax.numpy as jnp

    def _L0_rec_ref(dense_features, sparse_values):
        import jax, jax.numpy as jnp
        import numpy as np
        B, F, D = (2048, 26, 128)
        sd = jnp.einsum('bfd,bd->bf', sparse_values, dense_features)
        ss = jnp.einsum('bfd,bgd->bfg', sparse_values, sparse_values)
        iu, ju = jnp.triu_indices(F, k=1)
        pairs = ss[:, iu, ju]
        return jnp.concatenate([dense_features, sd, pairs], axis=1)
    e = jnp.stack([tbl_0[ids[:, 0]], tbl_1[ids[:, 1]], tbl_2[ids[:, 2]], tbl_3[ids[:, 3]], tbl_4[ids[:, 4]], tbl_5[ids[:, 5]], tbl_6[ids[:, 6]], tbl_7[ids[:, 7]], tbl_8[ids[:, 8]], tbl_9[ids[:, 9]], tbl_10[ids[:, 10]], tbl_11[ids[:, 11]], tbl_12[ids[:, 12]], tbl_13[ids[:, 13]], tbl_14[ids[:, 14]], tbl_15[ids[:, 15]], tbl_16[ids[:, 16]], tbl_17[ids[:, 17]], tbl_18[ids[:, 18]], tbl_19[ids[:, 19]], tbl_20[ids[:, 20]], tbl_21[ids[:, 21]], tbl_22[ids[:, 22]], tbl_23[ids[:, 23]], tbl_24[ids[:, 24]], tbl_25[ids[:, 25]]], axis=1)
    z = _L0_rec_ref(r_dense_features, e)
    z = z.reshape(z.shape[0], -1)
    h = jnp.concatenate([z, r_dense_features], axis=1)
    h = jnp.maximum(h @ W_top1 + b_top1, 0.0)
    h = jnp.maximum(h @ W_top2 + b_top2, 0.0)
    y = h @ W_top3
    return y

_drawn_inputs = setup_inputs


def setup_inputs(seed=0):
    import zlib

    import numpy as np

    out = dict(_drawn_inputs(seed))
    spreads = {'b_top1': (0.0, 0.1), 'b_top2': (0.0, 0.1)}
    factors = {}
    for name, (base, spread) in spreads.items():
        noise = np.random.default_rng([zlib.crc32(name.encode()), seed]).standard_normal(out[name].shape)
        drawn = base * np.exp(spread * noise) if base else spread * noise
        out[name] = jnp.asarray(drawn.astype(out[name].dtype))
    for name, factor in factors.items():
        out[name] = (out[name] * factor).astype(out[name].dtype)
    return out
```

```python
import concourse.bass as bass
from concourse import mybir
from concourse.alu_op_type import AluOpType as ALU
from contextlib import ExitStack

P = 128
BATCH, F, D = 512, 26, 128
H1, H2 = 512, 256
TILES = BATCH // P
TABLE_ROWS = [12500, 1250, 125000, 1000, 12500, 1250, 1250, 1000, 12500, 1000, 1250, 12500, 1250,
              1250, 1000, 1000, 1250, 12500, 1250, 1250, 12500, 12500, 1000, 1000, 1250, 1250]
ROWS = 1000
ONEHOT = [f for f in range(F) if TABLE_ROWS[f] == ROWS]
GATHERED = [f for f in range(F) if f not in ONEHOT]
SLOT_FEATURE = [None] + ONEHOT + GATHERED
SLOTS = len(SLOT_FEATURE)
WIDTH = 32
FIRST_GATHERED = 1 + len(ONEHOT)

FULL = ROWS // P
REST = ROWS - FULL * P
CHUNKS = FULL + 1
PARTS = 3

TABLE_SLOTS = 3
GROUP = 4
GROUPS = [list(range(g, min(g + GROUP, len(GATHERED)))) for g in range(0, len(GATHERED), GROUP)]

QUAD = 4
QUADS = P // QUAD
UNIT = 8
UNITS = QUADS // UNIT
MOVING = SLOTS - 1
JJ = 28
R = 4
BLOCKS = JJ // R
CUTS = [(0, 3, 12), (3, 2, 20), (5, 2, 26)]
PAIR_ROWS = sum(n * w for _, n, w in CUTS)


def pair_row_places():
    def source(i, j):
        a, b = SLOT_FEATURE[i], SLOT_FEATURE[j]
        if a is None:
            return D + b
        a, b = min(a, b), max(a, b)
        return D + F + a * (F - 1) - a * (a - 1) // 2 + (b - a - 1)
    out, at = [[] for _ in range(R)], 0
    for first, n, width in CUTS:
        for block in range(first, first + n):
            for i in range(width):
                for r in range(R):
                    jj = R * block + r
                    if i <= jj < MOVING:
                        out[r].append((at, source(i, jj + 1)))
                at += 1
    return out


def schedule():
    groups = [("group", c, g) for c in range(TILES) for g in range(len(GROUPS))]
    out = [("prepare", 0, 0), ("dense", 0, 0), ("prepare", 1, 0)]
    n = len(ONEHOT)
    for t in range(n):
        out.append(("onehot", t, 0))
        if t + 2 < n:
            out.append(("prepare", t + 2, 0))
        if t >= 1:
            out.append(groups.pop(0))
    def take(k):
        for _ in range(min(k, len(groups))):
            out.append(groups.pop(0))
    per = len(GROUPS)
    take(1)
    units = lambda c: [("dots", c, u) for u in range(UNITS)]
    for c in range(TILES):
        if c == 0:
            out.extend(units(0))
            take(2 * per - (len(GROUPS) * TILES - len(groups)))
            nxt = units(1)
        elif c == 1:
            nxt = groups[:4]
            del groups[:4]
        elif c == 2:
            take(1)
            out.extend(units(2))
            nxt = groups[:4]
            del groups[:4]
        else:
            take(1)
            out.extend(units(3))
            nxt = []
        for stage in ("swap", "pairs", "hidden1", "hidden2"):
            out.append((stage, c, 0))
            if nxt:
                out.append(nxt.pop(0))
        out.append(("score", c, 0))
    assert not groups
    return out


SCHEDULE = schedule()
RING = 2
FEATURE_ITEMS = [s for s in SCHEDULE if s[0] in ("dense", "onehot", "group")]


def evacuator(item):
    kind, c, g = item
    if kind == "dense":
        return "vector"
    if kind == "onehot" or c == 0:
        return "scalar"
    return "vector" if g % 2 else "scalar"


def looked_up(t):
    return FEATURE_ITEMS.index(("onehot", t, 0)) + 1


def evacuated(item, back=0):
    n = FEATURE_ITEMS.index(item) - back
    if n < 0:
        return None
    who = evacuator(FEATURE_ITEMS[n])
    return who, sum(evacuator(x) == who for x in FEATURE_ITEMS[:n + 1])


def before(item):
    done = [x for x in SCHEDULE[:SCHEDULE.index(item)] if x in FEATURE_ITEMS]
    return {who: sum(evacuator(x) == who for x in done) for who in ("vector", "scalar")}


def dlrm_tower(nc, ids_dram, dense_dram, onehot_ids_dram, tables, w1_dram, w2_dram, small_dram, out):
    F32, BF16, F16, I32 = mybir.dt.float32, mybir.dt.bfloat16, mybir.dt.float16, mybir.dt.int32
    ACT = mybir.ActivationFunctionType
    ctx = ExitStack()
    with ctx:
        def sb(name, shape, dt):
            return ctx.enter_context(nc.sbuf_tensor(name, shape, dt))

        def sem(name):
            return ctx.enter_context(nc.semaphore(name))

        nt = len(ONEHOT)
        ids = sb("ids", [P, TILES * F], I32)
        dense = sb("dense", [P, TILES, D], F32)
        gathered = sb("gathered", [P, TILES, len(GATHERED), D], F32)
        ident = sb("ident", [P, P], F32)
        row_id = sb("row_id", [P, CHUNKS], F32)
        id_words = sb("id_words", [P, 2, BATCH], I32)
        id_half = sb("id_half", [P, 2, BATCH], F16)
        table = sb("table", [P, TABLE_SLOTS, CHUNKS, D], F32)
        rest = sb("rest", [P, CHUNKS, D], F32)
        parts = sb("parts", [P, 2, PARTS, CHUNKS, D], BF16)
        hot = sb("hot", [P, 2, CHUNKS, BATCH], BF16)
        feat = sb("feat", [P, BATCH, WIDTH], F32)
        dense_t = sb("dense_t", [P, BATCH], F32)
        dots = sb("dots", [P, 2, JJ, QUADS], F32)
        swapped = sb("swapped", [P, 2, QUAD, PAIR_ROWS], F32)
        pairs = sb("pairs", [P, 2, R, P], F32)
        h1 = sb("h1", [P, H1 // P, BATCH], F32)
        h2 = sb("h2", [P, H2 // P, BATCH], F32)
        w1 = sb("w1", [P, R + 2, H1], F32)
        w1_dense = sb("w1_dense", [P, H1], F32)
        w2 = sb("w2", [P, H1 // P, H2], F32)
        small = sb("small", [P, 8], F32)
        y = sb("y", [1, BATCH], F32)

        ring = [ctx.enter_context(nc.psum_tensor(f"ring{i}", [P, 512], F32)) for i in range(RING)]
        dot_banks = [ctx.enter_context(nc.psum_tensor(f"dots{i}", [P, 1024], F32)) for i in range(2)]
        bank_a = ctx.enter_context(nc.psum_tensor("bank_a", [P, 512], F32))
        bank_b = ctx.enter_context(nc.psum_tensor("bank_b", [P, 512], F32))

        ids_in, dense_in, small_in, w1_in, w2_in = (sem(n) for n in (
            "ids_in", "dense_in", "small_in", "w1_in", "w2_in"))
        ident_made, rows_made, ident_zero = sem("ident_made"), sem("rows_made"), sem("ident_zero")
        id_words_in = [sem(f"id_words_in{i}") for i in range(2)]
        id_half_made = sem("id_half_made")
        hot_made = sem("hot_made")
        table_in = [sem(f"table_in{i}") for i in range(TABLE_SLOTS)]
        high_made, rest_made, mid_made, low_made = (sem(n) for n in (
            "high_made", "rest_made", "mid_made", "low_made"))
        gather_in = [[sem(f"gather_in{c}_{g}") for g in range(len(GROUPS))] for c in range(TILES)]
        bank_full = sem("bank_full")
        feat_put = {"vector": sem("feat_put_vector"), "scalar": sem("feat_put_scalar")}
        pads_zero = sem("pads_zero")
        dots_full = sem("dots_full")
        dots_put = {"vector": sem("dots_put_vector"), "scalar": sem("dots_put_scalar")}
        w1_dense_made = sem("w1_dense_made")
        STAGES = ("swap", "pairs", "hidden1", "hidden2")
        a_full = {s: sem(f"{s}_a_full") for s in STAGES}
        b_full = {s: sem(f"{s}_b_full") for s in STAGES}
        a_put = {s: sem(f"{s}_a_put") for s in STAGES}
        b_put = {s: sem(f"{s}_b_put") for s in STAGES}
        score_full, score_put, stored = sem("score_full"), sem("score_put"), sem("stored")

        block = ctx.enter_context(nc.Block())

        @block.sync
        def _(sp):
            sp.dma_start(ids[:, :], ids_dram).then_inc(ids_in, 16)
            sp.dma_start(dense[:, :, :], dense_dram.rearrange("(c p) d -> p c d", p=P)).then_inc(dense_in, 16)

            def load_ids(t):
                if t >= 2:
                    sp.wait_ge(id_half_made, t - 1)
                sp.dma_start(id_words[:, t % 2, :],
                             onehot_ids_dram[t:t + 1, :].broadcast_to([P, BATCH])).then_inc(id_words_in[t % 2], 16)

            def load_table(t):
                if t >= TABLE_SLOTS:
                    sp.wait_ge(rest_made, t - TABLE_SLOTS + 1)
                src = tables[ONEHOT[t]]
                sp.dma_start(table[:, t % TABLE_SLOTS, 0:FULL, :],
                             src[0:FULL * P, :].rearrange("(p n) d -> p n d", n=FULL)).then_inc(table_in[t % TABLE_SLOTS], 16)
                sp.dma_start(table[0:REST, t % TABLE_SLOTS, FULL, :], src[FULL * P:ROWS, :]).then_inc(table_in[t % TABLE_SLOTS], 16)

            load_ids(0)
            load_table(0)
            load_ids(1)
            load_table(1)
            load_ids(2)
            load_table(2)
            sp.dma_start(w1[:, :, :], w1_dram).then_inc(w1_in, 16)
            for t in range(3, nt):
                load_ids(t)
                load_table(t)
            sp.dma_start(small[:, :], small_dram).then_inc(small_in, 16)
            sp.dma_start(w2[:, :, :], w2_dram.rearrange("(k p) n -> p k n", p=P)).then_inc(w2_in, 16)
            sp.wait_ge(score_put, TILES)
            sp.dma_start(out, y[0:1, :]).then_inc(stored, 16)
            sp.wait_ge(stored, 16)

        @block.gpsimd
        def _(pool):
            nc.gpsimd.memset(ident[:, :], 0.0).then_inc(ident_zero, 1)
            pool.wait_ge(ident_zero, 1)
            nc.gpsimd.affine_select(out=ident[:, :], in_=ident[:, :], compare_op=ALU.not_equal, fill=1.0,
                                    base=0, pattern=[[-1, P]], channel_multiplier=1).then_inc(ident_made, 1)
            nc.gpsimd.iota(row_id[:, 0:FULL], pattern=[[1, FULL]], base=0, channel_multiplier=FULL,
                           allow_small_or_imprecise_dtypes=True).then_inc(rows_made, 1)
            nc.gpsimd.iota(row_id[:, FULL:CHUNKS], pattern=[[1, 1]], base=FULL * P, channel_multiplier=1,
                           allow_small_or_imprecise_dtypes=True).then_inc(rows_made, 1)
            pool.wait_ge(ids_in, 16)
            for c in range(TILES):
                for g, members in enumerate(GROUPS):
                    for m in members:
                        f = GATHERED[m]
                        nc.gpsimd.indirect_dma_start(
                            out=gathered[:, c, m, :], out_offset=None, in_=tables[f],
                            in_offset=bass.IndirectOffsetOnAxis(ap=ids[:, c * F + f:c * F + f + 1], axis=0),
                        ).then_inc(gather_in[c][g], 16)

        def put_features(engine, copy, item, n):
            kind, c, g = item
            bank = ring[n % RING]
            engine.wait_ge(bank_full, n + 1)
            if kind == "dense":
                copy(dense_t[:, :], bank[:, :])
                last = copy(feat[:, :, 0], bank[:, :])
            elif kind == "onehot":
                last = copy(feat[:, :, 1 + c], bank[:, :])
            else:
                s, w = FIRST_GATHERED + GROUPS[g][0], len(GROUPS[g])
                last = copy(feat[:, c * P:(c + 1) * P, s:s + w],
                            bank[:, 0:w * P].rearrange("p (s b) -> p b s", s=w))
            last.then_inc(feat_put[evacuator(item)], 1)

        def put_dots(engine, copy, c, u, quarters, who):
            n = c * UNITS + u
            engine.wait_ge(dots_full, n + 1)
            if c >= 2 and u == 0:
                engine.wait_ge(a_full["swap"], c - 1)
                engine.wait_ge(b_full["swap"], c - 1)
            src = dot_banks[n % 2][:, :].rearrange("p (q m) -> p q m", q=UNIT)
            for k in quarters:
                part = slice(WIDTH * k, WIDTH * (k + 1))
                last = copy(dots[part, c % 2, 0:MOVING, UNIT * u:UNIT * (u + 1)],
                            src[part, :, k * MOVING:(k + 1) * MOVING].rearrange("p q m -> p m q"))
            last.then_inc(dots_put[who], 1)

        def put_swapped(copy, c, cut, bank, first_block, offset):
            first, n, width = cut
            src = bank[:, :].rearrange("p (b k i) -> p k b i", k=QUAD, i=WIDTH)
            dst = swapped[:, c % 2, :, offset:offset + n * width].rearrange("p k (b i) -> p k b i", i=width)
            return copy(dst, src[:, :, first - first_block:first - first_block + n, 0:width])

        def put_pairs(copy, c, bank, half):
            dst = pairs[:, c % 2, :, :].rearrange("p r (q k) -> p k r q", k=QUAD)[:, 2 * half:2 * half + 2]
            src = bank[:, 0:2 * P].rearrange("p (k r q) -> p k r q", k=2, r=R)
            for k in range(2):
                last = copy(dst[:, k], src[:, k])
            return last

        @block.scalar
        def _(act):
            def relu(dst, src, bias):
                return nc.scalar.activation(dst, src, ACT.Relu, bias=bias)

            for item in SCHEDULE:
                kind, c, g = item
                if kind == "prepare":
                    act.wait_ge(id_words_in[c % 2], 16 * (c // 2 + 1))
                    if c >= 2:
                        act.wait_ge(hot_made, c - 1)
                    nc.scalar.copy(id_half[:, c % 2, :], id_words[:, c % 2, :]).then_inc(id_half_made, 1)
                    act.wait_ge(table_in[c % TABLE_SLOTS], 32 * (c // TABLE_SLOTS + 1))
                    if c >= 2:
                        act.wait_ge(bank_full, looked_up(c - 2))
                    nc.scalar.copy(parts[:, c % 2, 0, 0:FULL, :], table[:, c % TABLE_SLOTS, 0:FULL, :])
                    nc.scalar.copy(parts[0:REST, c % 2, 0, FULL, :],
                                   table[0:REST, c % TABLE_SLOTS, FULL, :]).then_inc(high_made, 1)
                    act.wait_ge(rest_made, c + 1)
                    nc.scalar.copy(parts[:, c % 2, 1, 0:FULL, :], rest[:, 0:FULL, :])
                    nc.scalar.copy(parts[0:REST, c % 2, 1, FULL, :], rest[0:REST, FULL, :]).then_inc(mid_made, 1)
                elif item in FEATURE_ITEMS and evacuator(item) == "scalar":
                    put_features(act, nc.scalar.copy, item, FEATURE_ITEMS.index(item))
                elif kind == "dots":
                    put_dots(act, nc.scalar.copy, c, g, (0, 1), "scalar")
                elif kind == "swap":
                    act.wait_ge(a_full["swap"], c + 1)
                    put_swapped(nc.scalar.copy, c, CUTS[0], bank_a, 0, 0).then_inc(a_put["swap"], 1)
                elif kind == "pairs":
                    act.wait_ge(a_full["pairs"], c + 1)
                    put_pairs(nc.scalar.copy, c, bank_a, 0).then_inc(a_put["pairs"], 1)
                elif kind == "hidden1":
                    act.wait_ge(a_full["hidden1"], c + 1)
                    act.wait_ge(small_in, 16)
                    for n in range(2):
                        last = relu(h1[:, n, c * P:(c + 1) * P], bank_a[:, n * P:(n + 1) * P], small[:, n:n + 1])
                    last.then_inc(a_put["hidden1"], 1)
                elif kind == "hidden2":
                    act.wait_ge(a_full["hidden2"], c + 1)
                    relu(h2[:, 0, c * P:(c + 1) * P], bank_a[:, 0:P], small[:, 4:5]).then_inc(a_put["hidden2"], 1)

        @block.vector
        def _(dve):
            def relu(dst, src, bias):
                return nc.vector.tensor_scalar(dst, src, bias, 0.0, ALU.add, ALU.max)

            nc.vector.memset(feat[:, :, SLOTS:WIDTH], 0.0)
            nc.vector.memset(dots[:, :, MOVING:JJ, :], 0.0).then_inc(pads_zero, 1)
            for item in SCHEDULE:
                kind, c, g = item
                if kind == "prepare":
                    dve.wait_ge(id_half_made, c + 1)
                    if c == 0:
                        dve.wait_ge(rows_made, 2)
                    if c >= 2:
                        dve.wait_ge(bank_full, looked_up(c - 2))
                    for n in range(CHUNKS):
                        k = P if n < FULL else REST
                        last = nc.vector.tensor_scalar(hot[0:k, c % 2, n, :], id_half[0:k, c % 2, :],
                                                       row_id[0:k, n:n + 1], None, ALU.is_equal)
                    last.then_inc(hot_made, 1)
                    dve.wait_ge(high_made, c + 1)
                    if c >= 1:
                        dve.wait_ge(low_made, c)
                    nc.vector.tensor_tensor(rest[:, 0:FULL, :], table[:, c % TABLE_SLOTS, 0:FULL, :],
                                            parts[:, c % 2, 0, 0:FULL, :], ALU.subtract)
                    nc.vector.tensor_tensor(rest[0:REST, FULL, :], table[0:REST, c % TABLE_SLOTS, FULL, :],
                                            parts[0:REST, c % 2, 0, FULL, :], ALU.subtract).then_inc(rest_made, 1)
                    dve.wait_ge(mid_made, c + 1)
                    nc.vector.tensor_tensor(parts[:, c % 2, 2, 0:FULL, :], rest[:, 0:FULL, :],
                                            parts[:, c % 2, 1, 0:FULL, :], ALU.subtract)
                    nc.vector.tensor_tensor(parts[0:REST, c % 2, 2, FULL, :], rest[0:REST, FULL, :],
                                            parts[0:REST, c % 2, 1, FULL, :], ALU.subtract).then_inc(low_made, 1)
                elif item in FEATURE_ITEMS and evacuator(item) == "vector":
                    put_features(dve, nc.vector.tensor_copy, item, FEATURE_ITEMS.index(item))
                elif kind == "dots":
                    put_dots(dve, nc.vector.tensor_copy, c, g, (2, 3), "vector")
                elif kind == "swap":
                    if c == 0:
                        dve.wait_ge(w1_in, 16)
                        nc.vector.tensor_tensor(w1_dense[:, :], w1[:, R, :], w1[:, R + 1, :],
                                                ALU.add).then_inc(w1_dense_made, 1)
                    dve.wait_ge(b_full["swap"], c + 1)
                    at = CUTS[0][1] * CUTS[0][2]
                    put_swapped(nc.vector.tensor_copy, c, CUTS[1], bank_b, 3, at)
                    at += CUTS[1][1] * CUTS[1][2]
                    put_swapped(nc.vector.tensor_copy, c, CUTS[2], bank_b, 3, at).then_inc(b_put["swap"], 1)
                elif kind == "pairs":
                    dve.wait_ge(b_full["pairs"], c + 1)
                    put_pairs(nc.vector.tensor_copy, c, bank_b, 1).then_inc(b_put["pairs"], 1)
                elif kind == "hidden1":
                    dve.wait_ge(b_full["hidden1"], c + 1)
                    dve.wait_ge(small_in, 16)
                    for n in range(2):
                        last = relu(h1[:, 2 + n, c * P:(c + 1) * P], bank_b[:, n * P:(n + 1) * P],
                                    small[:, 2 + n:3 + n])
                    last.then_inc(b_put["hidden1"], 1)
                elif kind == "hidden2":
                    dve.wait_ge(b_full["hidden2"], c + 1)
                    relu(h2[:, 1, c * P:(c + 1) * P], bank_b[:, 0:P], small[:, 5:6]).then_inc(b_put["hidden2"], 1)
                elif kind == "score":
                    dve.wait_ge(score_full, c + 1)
                    nc.vector.tensor_copy(y[0:1, c * P:(c + 1) * P], bank_a[0:1, 0:P]).then_inc(score_put, 1)

        @block.tensor
        def _(pe):
            for item in SCHEDULE:
                kind, c, g = item
                cols = slice(c * P, (c + 1) * P)
                if item in FEATURE_ITEMS:
                    n = FEATURE_ITEMS.index(item)
                    bank = ring[n % RING]
                    free = evacuated(item, RING)
                    if free:
                        pe.wait_ge(feat_put[free[0]], free[1])
                if kind == "dense":
                    pe.wait_ge(ident_made, 1)
                    pe.wait_ge(dense_in, 16)
                    for t in range(TILES):
                        last = nc.tensor.transpose(bank[:, t * P:(t + 1) * P], dense[:, t, :], ident[:, :])
                    last.then_inc(bank_full, 1)
                elif kind == "onehot":
                    pe.wait_ge(hot_made, c + 1)
                    pe.wait_ge(high_made, c + 1)
                    for part in range(PARTS):
                        if part == 1:
                            pe.wait_ge(mid_made, c + 1)
                        if part == 2:
                            pe.wait_ge(low_made, c + 1)
                        for n in range(CHUNKS):
                            k = P if n < FULL else REST
                            last = nc.tensor.matmul(bank[:, :], parts[0:k, c % 2, part, n, :], hot[0:k, c % 2, n, :],
                                                    start=(part == 0 and n == 0),
                                                    stop=(part == PARTS - 1 and n == CHUNKS - 1))
                    last.then_inc(bank_full, 1)
                elif kind == "group":
                    pe.wait_ge(gather_in[c][g], 16 * len(GROUPS[g]))
                    for s, m in enumerate(GROUPS[g]):
                        last = nc.tensor.transpose(bank[:, s * P:(s + 1) * P], gathered[:, c, m, :], ident[:, :])
                    last.then_inc(bank_full, 1)
                elif kind == "dots":
                    n = c * UNITS + g
                    if g == 0:
                        for who, count in before(item).items():
                            if count:
                                pe.wait_ge(feat_put[who], count)
                        if c == 0:
                            pe.wait_ge(pads_zero, 1)
                    if n >= 2:
                        pe.wait_ge(dots_put["scalar"], n - 1)
                        pe.wait_ge(dots_put["vector"], n - 1)
                    for q in range(UNIT):
                        b = c * P + (g * UNIT + q) * QUAD
                        still = feat[:, b:b + QUAD, :].rearrange("p b s -> p (b s)")
                        last = nc.tensor.matmul(dot_banks[n % 2][:, q * P:q * P + QUAD * MOVING], still,
                                                feat[:, b:b + QUAD, 1:SLOTS], start=True, stop=True)
                    last.then_inc(dots_full, 1)
                elif kind == "swap":
                    pe.wait_ge(dots_put["scalar"], (c + 1) * UNITS)
                    pe.wait_ge(dots_put["vector"], (c + 1) * UNITS)
                    if c >= 1:
                        pe.wait_ge(score_put, c)
                        pe.wait_ge(b_put["hidden2"], c)
                    for j in range(BLOCKS):
                        bank, at = (bank_a, j) if j < 3 else (bank_b, j - 3)
                        last = nc.tensor.transpose(bank[:, at * P:(at + 1) * P],
                                                   dots[:, c % 2, R * j:R * (j + 1), :].rearrange("p r q -> p (r q)"),
                                                   ident[:, :])
                        if j == 2:
                            last.then_inc(a_full["swap"], 1)
                    last.then_inc(b_full["swap"], 1)
                elif kind == "pairs":
                    pe.wait_ge(a_put["swap"], c + 1)
                    pe.wait_ge(b_put["swap"], c + 1)
                    for k in range(QUAD):
                        bank, full = (bank_a, a_full) if k < 2 else (bank_b, b_full)
                        last = nc.tensor.transpose(bank[:, (k % 2) * P:(k % 2 + 1) * P],
                                                   swapped[:, c % 2, k, :], ident[:, :])
                        if k % 2:
                            last.then_inc(full["pairs"], 1)
                elif kind == "hidden1":
                    if c == 0:
                        pe.wait_ge(w1_dense_made, 1)
                    pe.wait_ge(a_put["pairs"], c + 1)
                    pe.wait_ge(b_put["pairs"], c + 1)
                    for n in range(H1 // P):
                        bank, full = (bank_a, a_full) if n < 2 else (bank_b, b_full)
                        dst = bank[:, (n % 2) * P:(n % 2 + 1) * P]
                        ns = slice(n * P, (n + 1) * P)
                        nc.tensor.matmul(dst, w1_dense[:, ns], dense_t[:, cols], start=True, stop=False)
                        for r in range(R):
                            last = nc.tensor.matmul(dst, w1[:, r, ns], pairs[:, c % 2, r, :],
                                                    start=False, stop=(r == R - 1))
                        if n % 2:
                            last.then_inc(full["hidden1"], 1)
                elif kind == "hidden2":
                    if c == 0:
                        pe.wait_ge(w2_in, 16)
                    pe.wait_ge(a_put["hidden1"], c + 1)
                    pe.wait_ge(b_put["hidden1"], c + 1)
                    for m in range(H2 // P):
                        bank, full = (bank_a, a_full) if m == 0 else (bank_b, b_full)
                        for n in range(H1 // P):
                            last = nc.tensor.matmul(bank[:, 0:P], w2[:, n, m * P:(m + 1) * P], h1[:, n, cols],
                                                    start=(n == 0), stop=(n == H1 // P - 1))
                        last.then_inc(full["hidden2"], 1)
                elif kind == "score":
                    pe.wait_ge(a_put["hidden2"], c + 1)
                    pe.wait_ge(b_put["hidden2"], c + 1)
                    for m in range(H2 // P):
                        last = nc.tensor.matmul(bank_a[0:1, 0:P], small[:, 6 + m:7 + m], h2[:, m, cols],
                                                start=(m == 0), stop=(m == H2 // P - 1))
                    last.then_inc(score_full, 1)


def kernel(**inputs):
    import numpy as np
    import concourse.bacc as bacc
    from concourse.bass_utils import run_bass_kernel_spmd as run

    x = {name: np.asarray(a) for name, a in inputs.items()}
    w1 = x["W_top1"]
    w1_tiles = np.zeros((P, R + 2, H1), w1.dtype)
    for r, places in enumerate(pair_row_places()):
        for place, row in places:
            w1_tiles[place, r] = w1[row]
    w1_tiles[:, R] = w1[0:D]
    w1_tiles[:, R + 1] = w1[w1.shape[0] - D:]
    small = np.concatenate([x["b_top1"].reshape(-1, P).T, x["b_top2"].reshape(-1, P).T,
                            x["W_top3"].reshape(-1, P).T], axis=1)
    arrays = {
        "ids": x["ids"].reshape(TILES, P, F).transpose(1, 0, 2).reshape(P, TILES * F),
        "dense": x["r_dense_features"],
        "onehot_ids": x["ids"].T[ONEHOT],
        "w1": w1_tiles, "w2": x["W_top2"], "small": small,
    }
    arrays.update({f"tbl_{f}": x[f"tbl_{f}"] for f in range(F)})
    arrays = {name: np.ascontiguousarray(a) for name, a in arrays.items()}

    nc = bacc.Bacc("TRN2", target_bir_lowering=False, num_devices=1)
    ap = {name: nc.dram_tensor("in_" + name, a.shape, mybir.dt.from_np(a.dtype), kind="ExternalInput").ap()
          for name, a in arrays.items()}
    out = nc.dram_tensor("scores", (BATCH, 1), mybir.dt.float32, kind="ExternalOutput").ap()
    dlrm_tower(nc, ap["ids"], ap["dense"], ap["onehot_ids"], [ap[f"tbl_{f}"] for f in range(F)],
               ap["w1"], ap["w2"], ap["small"], out.rearrange("b o -> o b"))
    result = run(nc, [{"in_" + name: a for name, a in arrays.items()}], core_ids=[0])
    return result.results[0]["scores"]
```

```python
import concourse.bass as bass
from concourse import mybir
from concourse.alu_op_type import AluOpType as ALU
from contextlib import ExitStack

P = 128
BATCH, F, D = 512, 26, 128
H1, H2 = 512, 256
TILES = BATCH // P
TABLE_ROWS = [12500, 1250, 125000, 1000, 12500, 1250, 1250, 1000, 12500, 1000, 1250, 12500, 1250,
              1250, 1000, 1000, 1250, 12500, 1250, 1250, 12500, 12500, 1000, 1000, 1250, 1250]
ROWS = 1000
LOOKUPS = 6
ONEHOT = [f for f in range(F) if TABLE_ROWS[f] == ROWS][:LOOKUPS]
LATE_TILE = 3
GATHERED = [f for f in range(F) if f not in ONEHOT]
SLOT_FEATURE = [None] + ONEHOT + GATHERED
LATE_SLOT = len(ONEHOT)
SLOTS = len(SLOT_FEATURE)
WIDTH = 32
FIRST_GATHERED = 1 + len(ONEHOT)

FULL = ROWS // P
REST = ROWS - FULL * P
CHUNKS = FULL + 1
SPANS = [(slice(0, FULL), P), (FULL, REST)]
PARTS = 3

TABLE_SLOTS = 3
WARM_UP = 8
GROUP = 4


def groups_of(tile):
    slots = list(range(FIRST_GATHERED if tile >= LATE_TILE else LATE_SLOT, SLOTS))
    out, end = [], []
    if tile == TILES - 1:
        end = [[slots.pop()]]
    while slots:
        n = GROUP - (len(slots) % GROUP > 0)
        out.append(slots[:n])
        del slots[:n]
    return out + end


GROUPS = [groups_of(c) for c in range(TILES)]


def lookup_columns(t):
    return slice(LATE_TILE * P if 1 + t == LATE_SLOT else 0, BATCH)



QUAD = 4
QUADS = P // QUAD
UNIT = 4
UNITS = QUADS // UNIT
MOVING = SLOTS - 1
JJ = 28
R = 4
BLOCKS = JJ // R
CUTS = [(0, 3, 12), (3, 2, 20), (5, 2, 26)]
PAIR_ROWS = sum(n * w for _, n, w in CUTS)


def pair_row_places():
    def source(i, j):
        a, b = SLOT_FEATURE[i], SLOT_FEATURE[j]
        if a is None:
            return D + b
        a, b = min(a, b), max(a, b)
        return D + F + a * (F - 1) - a * (a - 1) // 2 + (b - a - 1)
    out, at = [[] for _ in range(R)], 0
    for first, n, width in CUTS:
        for block in range(first, first + n):
            for i in range(width):
                for r in range(R):
                    jj = R * block + r
                    if i <= jj < MOVING:
                        out[r].append((at, source(i, jj + 1)))
                at += 1
    return out


def schedule():
    last = len(ONEHOT) - 1
    group = [[("group", c, g) for g in range(len(GROUPS[c]))] for c in range(TILES)]
    dots = [[("dots", c, u) for u in range(UNITS)] for c in range(TILES)]
    prepare = [("prepare", t, 0) for t in range(len(ONEHOT))]
    onehot = [("onehot", t, 0) for t in range(len(ONEHOT))]
    out = [prepare[0], prepare[1]]
    early = list(group[0])
    for t in range(last):
        out.append(onehot[t])
        if t + 2 < last:
            out.append(prepare[t + 2])
        if t == 0:
            out.append(("dense", 0, 0))
        else:
            out += early[:1]
            del early[:1]
        if t == 3:
            out.append(("fold", 0, 0))
    out += early
    for c in range(TILES):
        swap, pairs, hidden1, hidden2, score = (
            [(step, c, 0)] for step in ("swap", "pairs", "hidden1", "hidden2", "score"))
        scored = [("score", c - 1, 0)] if c else []
        out += dots[c]
        if c == TILES - 1:
            out += scored + [("hidden1_dense", c, 0)] + swap + pairs + hidden1 + hidden2 + score
            break
        g = group[c + 1]
        late = [onehot[last]] if c == LATE_TILE - 1 else []
        if c == TILES - 2:
            out += scored + g[0:1] + swap + late + pairs + g[1:3] + hidden1 + g[3:4] + hidden2 + g[4:]
        elif c:
            out += scored + g[0:1] + swap + g[1:3] + pairs + g[3:4]
            if c == LATE_TILE - 2:
                out.append(prepare[last])
            out += hidden1 + g[4:] + late + hidden2
        else:
            out += g[0:2] + swap + g[2:4] + pairs + g[4:5]
            if c == LATE_TILE - 2:
                out.append(prepare[last])
            out += hidden1 + g[5:] + hidden2
    return out


SCHEDULE = schedule()
LAST_TILE = TILES - 1
FEATURE_ITEMS = [s for s in SCHEDULE if s[0] in ("dense", "onehot", "group")]


def is_early_lookup(item):
    return item[0] == "onehot" and lookup_columns(item[1]).start == 0


RING = 3
RING_ITEMS = [s for s in FEATURE_ITEMS if not is_early_lookup(s)]
EARLY_LOOKUPS = [s for s in FEATURE_ITEMS if is_early_lookup(s)]


def evacuator(item):
    kind, c, g = item
    if kind == "onehot" or c == 0 and kind == "group":
        return "scalar"
    return "vector" if g % 2 or kind == "dense" else "scalar"


def evacuations(items):
    return {who: sum(evacuator(x) == who for x in items) for who in ("vector", "scalar")}


def last_user(item):
    line = EARLY_LOOKUPS if item in EARLY_LOOKUPS else RING_ITEMS
    n = line.index(item) - RING
    if n < 0:
        return None
    who = evacuator(line[n])
    return who, evacuations(FEATURE_ITEMS[:FEATURE_ITEMS.index(line[n]) + 1])[who]


def before(item):
    return evacuations([x for x in SCHEDULE[:SCHEDULE.index(item)] if x in FEATURE_ITEMS])


def dlrm_tower(nc, ids_dram, dense_dram, onehot_ids_dram, tables, w1_dram, w2_dram, small_dram, out):
    F32, BF16, F16, I32 = mybir.dt.float32, mybir.dt.bfloat16, mybir.dt.float16, mybir.dt.int32
    ACT = mybir.ActivationFunctionType
    ctx = ExitStack()
    with ctx:
        def sb(name, shape, dt):
            return ctx.enter_context(nc.sbuf_tensor(name, shape, dt))

        def sem(name):
            return ctx.enter_context(nc.semaphore(name))

        nt = len(ONEHOT)
        ids = sb("ids", [P, TILES * F], I32)
        dense = sb("dense", [P, TILES, D], F32)
        gathered = sb("gathered", [P, TILES, SLOTS - LATE_SLOT, D], F32)
        ident = sb("ident", [P, P], F32)
        row_id = sb("row_id", [P, CHUNKS], F32)
        id_words = sb("id_words", [P, 2, BATCH], I32)
        id_half = sb("id_half", [P, 2, BATCH], F16)
        table = sb("table", [P, TABLE_SLOTS, CHUNKS, D], F32)
        rest = sb("rest", [P, 2, CHUNKS, D], F32)
        low = sb("low", [P, 2, CHUNKS, D], BF16)
        hot = sb("hot", [P, 2, CHUNKS, BATCH], BF16)
        feat = sb("feat", [P, BATCH, WIDTH], F32)
        dense_t = sb("dense_t", [P, BATCH], F32)
        dots = sb("dots", [P, 2, JJ, QUADS], F32)
        swapped = sb("swapped", [P, 2, QUAD, PAIR_ROWS], F32)
        pairs = sb("pairs", [P, 2, R, P], F32)
        h1 = sb("h1", [P, H1 // P, BATCH], F32)
        h2 = sb("h2", [P, H2 // P, BATCH], F32)
        w1 = sb("w1", [P, R + 2, H1], F32)
        w1_dense = sb("w1_dense", [P, H1], F32)
        w2 = sb("w2", [P, H1 // P, H2], F32)
        small = sb("small", [P, 8], F32)
        y = sb("y", [1, BATCH], F32)

        ring = [ctx.enter_context(nc.psum_tensor(f"ring{i}", [P, 512], F32)) for i in range(RING)]
        dot_banks = [ctx.enter_context(nc.psum_tensor(f"dots{i}", [P, 512], F32)) for i in range(RING)]
        bank_a = ctx.enter_context(nc.psum_tensor("bank_a", [P, 512], F32))
        bank_b = ctx.enter_context(nc.psum_tensor("bank_b", [P, 512], F32))

        ids_in, dense_in, small_in, w1_in, w2_in = (sem(n) for n in (
            "ids_in", "dense_in", "small_in", "w1_in", "w2_in"))
        ident_made, rows_made, ident_zero = sem("ident_made"), sem("rows_made"), sem("ident_zero")
        id_words_in = [sem(f"id_words_in{i}") for i in range(2)]
        id_half_made = sem("id_half_made")
        hot_made = sem("hot_made")
        table_in = [sem(f"table_in{i}") for i in range(TABLE_SLOTS)]
        rest_made, low_made = sem("rest_made"), sem("low_made")
        gather_in = [[sem(f"gather_in{c}_{g}") for g in range(len(GROUPS[c]))] for c in range(TILES)]
        ring_full, lookup_full = sem("ring_full"), sem("lookup_full")
        feat_put = {"vector": sem("feat_put_vector"), "scalar": sem("feat_put_scalar")}
        pads_zero = sem("pads_zero")
        dots_full = sem("dots_full")
        dots_put = {"vector": sem("dots_put_vector"), "scalar": sem("dots_put_scalar")}
        w1_dense_made = sem("w1_dense_made")
        STAGES = ("swap", "pairs", "hidden1", "hidden2")
        a_full = {s: sem(f"{s}_a_full") for s in STAGES}
        b_full = {s: sem(f"{s}_b_full") for s in STAGES}
        a_put = {s: sem(f"{s}_a_put") for s in STAGES}
        b_put = {s: sem(f"{s}_b_put") for s in STAGES}
        score_full, score_put, stored = sem("score_full"), sem("score_put"), sem("stored")

        block = ctx.enter_context(nc.Block())

        @block.sync
        def _(sp):
            sp.dma_start(ids[:, :], ids_dram).then_inc(ids_in, 16)

            def load_ids(t):
                if t >= 2:
                    sp.wait_ge(id_half_made, t - 1)
                sp.dma_start(id_words[:, t % 2, :],
                             onehot_ids_dram[t:t + 1, :].broadcast_to([P, BATCH])).then_inc(id_words_in[t % 2], 16)

            def load_table(t):
                if t >= TABLE_SLOTS:
                    sp.wait_ge(rest_made, t - TABLE_SLOTS + 1)
                    sp.wait_ge(lookup_full, t - TABLE_SLOTS + 1)
                src = tables[ONEHOT[t]]
                sp.dma_start(table[:, t % TABLE_SLOTS, 0:FULL, :],
                             src[0:FULL * P, :].rearrange("(p n) d -> p n d", n=FULL)).then_inc(table_in[t % TABLE_SLOTS], 16)
                sp.dma_start(table[0:REST, t % TABLE_SLOTS, FULL, :], src[FULL * P:ROWS, :]).then_inc(table_in[t % TABLE_SLOTS], 16)

            load_ids(0)
            load_table(0)
            sp.dma_start(dense[:, :, :], dense_dram.rearrange("(c p) d -> p c d", p=P)).then_inc(dense_in, 16)
            load_ids(1)
            load_table(1)
            load_ids(2)
            load_table(2)
            sp.dma_start(w1[:, :, :], w1_dram).then_inc(w1_in, 16)
            for t in range(3, nt):
                load_ids(t)
                load_table(t)
            sp.dma_start(small[:, :], small_dram).then_inc(small_in, 16)
            sp.dma_start(w2[:, :, :], w2_dram.rearrange("(k p) n -> p k n", p=P)).then_inc(w2_in, 16)
            sp.wait_ge(score_put, TILES)
            sp.dma_start(out, y[0:1, :]).then_inc(stored, 16)
            sp.wait_ge(stored, 16)

        @block.gpsimd
        def _(pool):
            nc.gpsimd.memset(ident[:, :], 0.0).then_inc(ident_zero, 1)
            pool.wait_ge(ident_zero, 1)
            nc.gpsimd.affine_select(out=ident[:, :], in_=ident[:, :], compare_op=ALU.not_equal, fill=1.0,
                                    base=0, pattern=[[-1, P]], channel_multiplier=1).then_inc(ident_made, 1)
            nc.gpsimd.iota(row_id[:, 0:FULL], pattern=[[1, FULL]], base=0, channel_multiplier=FULL,
                           allow_small_or_imprecise_dtypes=True).then_inc(rows_made, 1)
            nc.gpsimd.iota(row_id[:, FULL:CHUNKS], pattern=[[1, 1]], base=FULL * P, channel_multiplier=1,
                           allow_small_or_imprecise_dtypes=True).then_inc(rows_made, 1)
            pool.wait_ge(ids_in, 16)
            for c in range(TILES):
                for g, slots in enumerate(GROUPS[c]):
                    for s in slots:
                        f = SLOT_FEATURE[s]
                        nc.gpsimd.indirect_dma_start(
                            out=gathered[:, c, s - LATE_SLOT, :], out_offset=None, in_=tables[f],
                            in_offset=bass.IndirectOffsetOnAxis(ap=ids[:, c * F + f:c * F + f + 1], axis=0),
                        ).then_inc(gather_in[c][g], 16)

        def top_half(words):
            if len(words.shape) == 3:
                return words.bitcast(BF16).rearrange("p n (d half) -> p n d half", half=2)[:, :, :, 1]
            return words.bitcast(BF16).rearrange("p (d half) -> p d half", half=2)[:, :, 1]

        def feature_bank(item):
            if item in EARLY_LOOKUPS:
                n = EARLY_LOOKUPS.index(item)
                return dot_banks[n % RING], lookup_full, n + 1
            n = RING_ITEMS.index(item)
            return ring[n % RING], ring_full, n + 1

        def hidden_banks(c):
            return (bank_a, bank_b) if c < LAST_TILE else (ring[0], ring[1])

        def score_bank(c):
            return bank_b if c < LAST_TILE else ring[1]

        def put_features(engine, copy, item):
            kind, c, g = item
            bank, full, count = feature_bank(item)
            engine.wait_ge(full, count)
            if kind == "dense":
                copy(dense_t[:, :], bank[:, 0:BATCH])
                last = copy(feat[:, :, 0], bank[:, 0:BATCH])
            elif kind == "onehot":
                cols = lookup_columns(c)
                last = copy(feat[:, cols, 1 + c], bank[:, cols])
            else:
                s, w = GROUPS[c][g][0], len(GROUPS[c][g])
                last = copy(feat[:, c * P:(c + 1) * P, s:s + w],
                            bank[:, 0:w * P].rearrange("p (s b) -> p b s", s=w))
            last.then_inc(feat_put[evacuator(item)], 1)

        def put_dots(engine, copy, c, u, quarters, who):
            n = c * UNITS + u
            engine.wait_ge(dots_full, n + 1)
            if c >= 2 and u == 0:
                engine.wait_ge(a_full["swap"], c - 1)
                engine.wait_ge(b_full["swap"], c - 1)
            src = dot_banks[n % RING][:, :].rearrange("p (q m) -> p q m", q=UNIT)
            for k in quarters:
                part = slice(WIDTH * k, WIDTH * (k + 1))
                last = copy(dots[part, c % 2, 0:MOVING, UNIT * u:UNIT * (u + 1)],
                            src[part, :, k * MOVING:(k + 1) * MOVING].rearrange("p q m -> p m q"))
            last.then_inc(dots_put[who], 1)

        def put_swapped(copy, c, cut, bank, first_block, offset):
            first, n, width = cut
            src = bank[:, :].rearrange("p (b k i) -> p k b i", k=QUAD, i=WIDTH)
            dst = swapped[:, c % 2, :, offset:offset + n * width].rearrange("p k (b i) -> p k b i", i=width)
            return copy(dst, src[:, :, first - first_block:first - first_block + n, 0:width])

        def put_pairs(copy, c, bank, half):
            dst = pairs[:, c % 2, :, :].rearrange("p r (q k) -> p k r q", k=QUAD)[:, 2 * half:2 * half + 2]
            src = bank[:, 0:2 * P].rearrange("p (k r q) -> p k r q", k=2, r=R)
            return copy(dst, src)

        @block.scalar
        def _(act):
            def relu(dst, src, bias):
                return nc.scalar.activation(dst, src, ACT.Relu, bias=bias)

            for item in SCHEDULE:
                kind, c, g = item
                if kind == "prepare":
                    act.wait_ge(id_words_in[c % 2], 16 * (c // 2 + 1))
                    if c >= 2:
                        act.wait_ge(hot_made, CHUNKS * (c - 1))
                    nc.scalar.copy(id_half[:, c % 2, :], id_words[:, c % 2, :]).then_inc(id_half_made, 1)
                elif item in FEATURE_ITEMS and evacuator(item) == "scalar":
                    put_features(act, nc.scalar.copy, item)
                elif kind == "dots":
                    put_dots(act, nc.scalar.copy, c, g, (0, 1), "scalar")
                elif kind == "swap":
                    act.wait_ge(a_full["swap"], c + 1)
                    put_swapped(nc.scalar.copy, c, CUTS[0], bank_a, 0, 0).then_inc(a_put["swap"], 1)
                elif kind == "pairs":
                    act.wait_ge(a_full["pairs"], c + 1)
                    put_pairs(nc.scalar.copy, c, bank_a, 0).then_inc(a_put["pairs"], 1)
                elif kind == "hidden1":
                    act.wait_ge(a_full["hidden1"], c + 1)
                    act.wait_ge(small_in, 16)
                    for n in range(2):
                        last = relu(h1[:, n, c * P:(c + 1) * P], hidden_banks(c)[0][:, n * P:(n + 1) * P], small[:, n:n + 1])
                    last.then_inc(a_put["hidden1"], 1)

        @block.vector
        def _(dve):
            def relu(dst, src, bias):
                return nc.vector.tensor_scalar(dst, src, bias, 0.0, ALU.add, ALU.max)

            nc.vector.memset(feat[:, :, SLOTS:WIDTH], 0.0)
            nc.vector.memset(dots[:, :, MOVING:JJ, :], 0.0).then_inc(pads_zero, 1)
            for item in SCHEDULE:
                kind, c, g = item
                if kind == "prepare":
                    dve.wait_ge(id_half_made, c + 1)
                    if c == 0:
                        dve.wait_ge(rows_made, 2)
                    if c >= 2:
                        dve.wait_ge(lookup_full, c - 1)
                    cols = lookup_columns(c)
                    for n in range(CHUNKS):
                        k = P if n < FULL else REST
                        nc.vector.tensor_scalar(hot[0:k, c % 2, n, cols], id_half[0:k, c % 2, cols],
                                                row_id[0:k, n:n + 1], None, ALU.is_equal).then_inc(hot_made, 1)
                    dve.wait_ge(table_in[c % TABLE_SLOTS], 32 * (c // TABLE_SLOTS + 1))
                    for n, k in SPANS:
                        last = nc.vector.tensor_tensor(rest[0:k, c % 2, n, :], table[0:k, c % TABLE_SLOTS, n, :],
                                                       top_half(table[0:k, c % TABLE_SLOTS, n, :]), ALU.subtract)
                    last.then_inc(rest_made, 1)
                    dve.wait_ge(rest_made, c + 1)
                    for n, k in SPANS:
                        last = nc.vector.tensor_tensor(low[0:k, c % 2, n, :], rest[0:k, c % 2, n, :],
                                                       top_half(rest[0:k, c % 2, n, :]), ALU.subtract)
                    last.then_inc(low_made, 1)
                elif item in FEATURE_ITEMS and evacuator(item) == "vector":
                    put_features(dve, nc.vector.tensor_copy, item)
                elif kind == "dots":
                    put_dots(dve, nc.vector.tensor_copy, c, g, (2, 3), "vector")
                elif kind == "fold":
                    dve.wait_ge(w1_in, 16)
                    nc.vector.tensor_tensor(w1_dense[:, :], w1[:, R, :], w1[:, R + 1, :],
                                            ALU.add).then_inc(w1_dense_made, 1)
                elif kind == "swap":
                    dve.wait_ge(b_full["swap"], c + 1)
                    at = CUTS[0][1] * CUTS[0][2]
                    put_swapped(nc.vector.tensor_copy, c, CUTS[1], bank_b, 3, at)
                    at += CUTS[1][1] * CUTS[1][2]
                    put_swapped(nc.vector.tensor_copy, c, CUTS[2], bank_b, 3, at).then_inc(b_put["swap"], 1)
                elif kind == "pairs":
                    dve.wait_ge(b_full["pairs"], c + 1)
                    put_pairs(nc.vector.tensor_copy, c, bank_b, 1).then_inc(b_put["pairs"], 1)
                elif kind == "hidden1":
                    dve.wait_ge(b_full["hidden1"], c + 1)
                    dve.wait_ge(small_in, 16)
                    for n in range(2):
                        last = relu(h1[:, 2 + n, c * P:(c + 1) * P], hidden_banks(c)[1][:, n * P:(n + 1) * P],
                                    small[:, 2 + n:3 + n])
                    last.then_inc(b_put["hidden1"], 1)
                elif kind == "hidden2":
                    dve.wait_ge(a_full["hidden2"], c + 1)
                    for m in range(H2 // P):
                        last = relu(h2[:, m, c * P:(c + 1) * P], hidden_banks(c)[0][:, m * P:(m + 1) * P],
                                    small[:, 4 + m:5 + m])
                    last.then_inc(a_put["hidden2"], 1)
                elif kind == "score":
                    dve.wait_ge(score_full, c + 1)
                    nc.vector.tensor_copy(y[0:1, c * P:(c + 1) * P], score_bank(c)[0:1, 0:P]).then_inc(score_put, 1)

        @block.tensor
        def _(pe):
            def first_layer(c, n, dense_part, pairs_part):
                dst = hidden_banks(c)[n // 2][:, (n % 2) * P:(n % 2 + 1) * P]
                ns = slice(n * P, (n + 1) * P)
                if dense_part:
                    last = nc.tensor.matmul(dst, w1_dense[:, ns], dense_t[:, c * P:(c + 1) * P],
                                            start=pairs_part or n % 2 == 0, stop=False, skip_group_check=True)
                if pairs_part:
                    for r in range(R):
                        last = nc.tensor.matmul(dst, w1[:, r, ns], pairs[:, c % 2, r, :],
                                                start=False, stop=(r == R - 1), skip_group_check=True)
                return last

            pe.wait_ge(ident_made, 1)
            for _ in range(WARM_UP):
                nc.tensor.matmul(bank_a[:, 0:P], ident[:, :], ident[:, :], start=True, stop=True)
            for item in SCHEDULE:
                kind, c, g = item
                cols = slice(c * P, (c + 1) * P)
                if item in FEATURE_ITEMS:
                    bank, full, _ = feature_bank(item)
                    free = last_user(item)
                    if free:
                        pe.wait_ge(feat_put[free[0]], free[1])
                if kind == "dense":
                    pe.wait_ge(dense_in, 16)
                    for t in range(TILES):
                        last = nc.tensor.transpose(bank[:, t * P:(t + 1) * P], dense[:, t, :], ident[:, :])
                    last.then_inc(full, 1)
                elif kind == "onehot":
                    pe.wait_ge(table_in[c % TABLE_SLOTS], 32 * (c // TABLE_SLOTS + 1))
                    cols = lookup_columns(c)
                    for part in range(PARTS):
                        if part == 1:
                            pe.wait_ge(rest_made, c + 1)
                        if part == 2:
                            pe.wait_ge(low_made, c + 1)
                        for n in range(CHUNKS):
                            k = P if n < FULL else REST
                            if part == 0:
                                pe.wait_ge(hot_made, CHUNKS * c + n + 1)
                                weights = top_half(table[0:k, c % TABLE_SLOTS, n, :])
                            elif part == 1:
                                weights = top_half(rest[0:k, c % 2, n, :])
                            else:
                                weights = low[0:k, c % 2, n, :]
                            last = nc.tensor.matmul(bank[:, cols], weights, hot[0:k, c % 2, n, cols],
                                                    start=(part == 0 and n == 0),
                                                    stop=(part == PARTS - 1 and n == CHUNKS - 1))
                    last.then_inc(full, 1)
                elif kind == "group":
                    pe.wait_ge(gather_in[c][g], 16 * len(GROUPS[c][g]))
                    for n, s in enumerate(GROUPS[c][g]):
                        last = nc.tensor.transpose(bank[:, n * P:(n + 1) * P], gathered[:, c, s - LATE_SLOT, :],
                                                   ident[:, :])
                    last.then_inc(full, 1)
                elif kind == "dots":
                    n = c * UNITS + g
                    if g == 0:
                        for who, count in before(item).items():
                            if count:
                                pe.wait_ge(feat_put[who], count)
                        if c == 0:
                            pe.wait_ge(pads_zero, 1)
                    if n >= RING:
                        pe.wait_ge(dots_put["scalar"], n - RING + 1)
                        pe.wait_ge(dots_put["vector"], n - RING + 1)
                    for q in range(UNIT):
                        b = c * P + (g * UNIT + q) * QUAD
                        still = feat[:, b:b + QUAD, :].rearrange("p b s -> p (b s)")
                        last = nc.tensor.matmul(dot_banks[n % RING][:, q * P:q * P + QUAD * MOVING], still,
                                                feat[:, b:b + QUAD, 1:SLOTS], start=True, stop=True)
                    last.then_inc(dots_full, 1)
                elif kind == "swap":
                    pe.wait_ge(dots_put["scalar"], (c + 1) * UNITS)
                    pe.wait_ge(dots_put["vector"], (c + 1) * UNITS)
                    for j in range(BLOCKS):
                        if c >= 1 and j == 0:
                            pe.wait_ge(a_put["hidden2"], c)
                        if c >= 1 and j == 3:
                            pe.wait_ge(score_put, c)
                        bank, at = (bank_a, j) if j < 3 else (bank_b, j - 3)
                        last = nc.tensor.transpose(bank[:, at * P:(at + 1) * P],
                                                   dots[:, c % 2, R * j:R * (j + 1), :].rearrange("p r q -> p (r q)"),
                                                   ident[:, :])
                        if j == 2:
                            last.then_inc(a_full["swap"], 1)
                    last.then_inc(b_full["swap"], 1)
                elif kind == "pairs":
                    pe.wait_ge(a_put["swap"], c + 1)
                    pe.wait_ge(b_put["swap"], c + 1)
                    for k in range(QUAD):
                        bank, full = (bank_a, a_full) if k < 2 else (bank_b, b_full)
                        last = nc.tensor.transpose(bank[:, (k % 2) * P:(k % 2 + 1) * P],
                                                   swapped[:, c % 2, k, :], ident[:, :])
                        if k % 2:
                            last.then_inc(full["pairs"], 1)
                elif kind == "hidden1_dense":
                    for n in range(H1 // P):
                        first_layer(c, n, True, False)
                elif kind == "hidden1":
                    if c == 0:
                        pe.wait_ge(w1_dense_made, 1)
                    pe.wait_ge(a_put["pairs"], c + 1)
                    pe.wait_ge(b_put["pairs"], c + 1)
                    for n in range(H1 // P):
                        last = first_layer(c, n, c < LAST_TILE, True)
                        if n == 1:
                            last.then_inc(a_full["hidden1"], 1)
                    last.then_inc(b_full["hidden1"], 1)
                elif kind == "hidden2":
                    if c == 0:
                        pe.wait_ge(w2_in, 16)
                    for half, put in enumerate((a_put, b_put)):
                        pe.wait_ge(put["hidden1"], c + 1)
                        for m in range(H2 // P):
                            for n in (2 * half, 2 * half + 1):
                                last = nc.tensor.matmul(hidden_banks(c)[0][:, m * P:(m + 1) * P],
                                                        w2[:, n, m * P:(m + 1) * P], h1[:, n, cols],
                                                        start=(m == 0 and n == 0), stop=(n == H1 // P - 1),
                                                        skip_group_check=True)
                    last.then_inc(a_full["hidden2"], 1)
                elif kind == "score":
                    pe.wait_ge(a_put["hidden2"], c + 1)
                    for m in range(H2 // P):
                        last = nc.tensor.matmul(score_bank(c)[0:1, 0:P], small[:, 6 + m:7 + m], h2[:, m, cols],
                                                start=(m == 0), stop=(m == H2 // P - 1))
                    last.then_inc(score_full, 1)


def kernel(**inputs):
    import numpy as np
    import concourse.bacc as bacc
    from concourse.bass_utils import run_bass_kernel_spmd as run

    x = {name: np.asarray(a) for name, a in inputs.items()}
    w1 = x["W_top1"]
    w1_tiles = np.zeros((P, R + 2, H1), w1.dtype)
    for r, places in enumerate(pair_row_places()):
        for place, row in places:
            w1_tiles[place, r] = w1[row]
    w1_tiles[:, R] = w1[0:D]
    w1_tiles[:, R + 1] = w1[w1.shape[0] - D:]
    small = np.concatenate([x["b_top1"].reshape(-1, P).T, x["b_top2"].reshape(-1, P).T,
                            x["W_top3"].reshape(-1, P).T], axis=1)
    arrays = {
        "ids": x["ids"].reshape(TILES, P, F).transpose(1, 0, 2).reshape(P, TILES * F),
        "dense": x["r_dense_features"],
        "onehot_ids": x["ids"].T[ONEHOT],
        "w1": w1_tiles, "w2": x["W_top2"], "small": small,
    }
    arrays.update({f"tbl_{f}": x[f"tbl_{f}"] for f in range(F)})
    arrays = {name: np.ascontiguousarray(a) for name, a in arrays.items()}

    nc = bacc.Bacc("TRN2", target_bir_lowering=False, num_devices=1)
    ap = {name: nc.dram_tensor("in_" + name, a.shape, mybir.dt.from_np(a.dtype), kind="ExternalInput").ap()
          for name, a in arrays.items()}
    out = nc.dram_tensor("scores", (BATCH, 1), mybir.dt.float32, kind="ExternalOutput").ap()
    dlrm_tower(nc, ap["ids"], ap["dense"], ap["onehot_ids"], [ap[f"tbl_{f}"] for f in range(F)],
               ap["w1"], ap["w2"], ap["small"], out.rearrange("b o -> o b"))
    result = run(nc, [{"in_" + name: a for name, a in arrays.items()}], core_ids=[0])
    return result.results[0]["scores"]
```

```python
import concourse.bass as bass
from concourse import mybir
from concourse.alu_op_type import AluOpType as ALU
from contextlib import ExitStack

P = 128
BATCH, F, D = 512, 26, 128
H1, H2 = 512, 256
TILES = BATCH // P
TABLE_ROWS = [12500, 1250, 125000, 1000, 12500, 1250, 1250, 1000, 12500, 1000, 1250, 12500, 1250,
              1250, 1000, 1000, 1250, 12500, 1250, 1250, 12500, 12500, 1000, 1000, 1250, 1250]
ROWS = 1000
LOOKUPS = 7
ONEHOT = [f for f in range(F) if TABLE_ROWS[f] == ROWS][:LOOKUPS]
LATE_TILE = 2
GATHERED = [f for f in range(F) if f not in ONEHOT]
SLOT_FEATURE = [None] + ONEHOT + GATHERED
LATE_SLOT = len(ONEHOT)
SLOTS = len(SLOT_FEATURE)
WIDTH = 32
FIRST_GATHERED = 1 + len(ONEHOT)

FULL = ROWS // P
REST = ROWS - FULL * P
CHUNKS = FULL + 1
SPANS = [(slice(0, FULL), P), (FULL, REST)]
PARTS = 3

TABLE_SLOTS = 3
WARM_UP = 8
GROUP = 4


def groups_of(tile):
    slots = list(range(FIRST_GATHERED if tile >= LATE_TILE else LATE_SLOT, SLOTS))
    out, end = [], []
    if tile == TILES - 1:
        end = [[slots.pop()]]
    while slots:
        n = GROUP - (len(slots) % GROUP > 0)
        out.append(slots[:n])
        del slots[:n]
    return out + end


GROUPS = [groups_of(c) for c in range(TILES)]


def lookup_columns(t):
    return slice(LATE_TILE * P if 1 + t == LATE_SLOT else 0, BATCH)



QUAD = 4
QUADS = P // QUAD
UNIT = 4
UNITS = QUADS // UNIT
MOVING = SLOTS - 1
CUTS = [(0, 1, 1), (1, 3, 4), (4, 3, 7), (7, 3, 10), (10, 4, 14), (14, 4, 18), (18, 4, 22), (22, 4, 26)]
CUT_CELL = [sum(n * w for _, n, w in CUTS[:cut]) for cut in range(len(CUTS) + 1)]
CHUNKS_OF_PAIRS = CUT_CELL[-1] // P
HIGH_CUTS, LOW_CUTS = [7, 6, 5], [4, 3, 2, 1, 0]
HIGH = CUTS[HIGH_CUTS[-1]][0]


def pair_row_places():
    def source(i, j):
        a, b = SLOT_FEATURE[i], SLOT_FEATURE[j]
        if a is None:
            return D + b
        a, b = min(a, b), max(a, b)
        return D + F + a * (F - 1) - a * (a - 1) // 2 + (b - a - 1)
    return [(CUT_CELL[cut] + (jj - first) * width + i, source(i, jj + 1))
            for cut, (first, n, width) in enumerate(CUTS)
            for jj in range(first, first + n) for i in range(jj + 1)]


def schedule():
    last = len(ONEHOT) - 1
    groups = [[("group", c, g) for g in range(len(GROUPS[c]))] for c in range(TILES)]
    prepare = [("prepare", t, 0) for t in range(len(ONEHOT))]
    onehot = [("onehot", t, 0) for t in range(len(ONEHOT))]
    out = [prepare[0], prepare[1]]
    waiting = groups[0][:]

    def take(n):
        out.extend(waiting[:n])
        del waiting[:n]

    for t in range(last):
        out.append(onehot[t])
        if t + 2 <= last:
            out.append(prepare[t + 2])
        if t == 0:
            out.append(("dense", 0, 0))
        else:
            take(1)
        if t == 3:
            out.append(("fold", 0, 0))
    take(len(waiting))
    waiting = [g for tile in groups[1:] for g in tile]
    take(FILL[0])
    for c in range(TILES):
        out += [("dots", c, u) for u in range(UNITS)] + [("pack", c, 0)]
        if c:
            out.append(("hidden2", c - 1, 0))
        if c == LAST_TILE:
            out.append(("hidden1_dense", c, 0))
        if c == 0:
            out.append(onehot[last])
        take(FILL[1] if c else FILL[2])
        out.append(("pairs", c, 0))
        if c:
            out.append(("score", c - 1, 0))
        take(FILL[3] if c else FILL[4])
        out.append(("hidden1", c, 0))
        if c < LAST_TILE:
            end = sum(len(tile) for tile in groups[c + 2:])
            take(max(0, len(waiting) - end))
        out.append(("hidden1", c, 1))
    return out + [("hidden2", LAST_TILE, 0), ("score", LAST_TILE, 0)]


FILL = [2, 2, 2, 2, 1]
LAST_TILE = TILES - 1
SCHEDULE = schedule()
PASSING = [s for s in SCHEDULE if s[0] in ("onehot", "group", "score")]


def is_early_lookup(item):
    return item[0] == "onehot" and lookup_columns(item[1]).start == 0


RING = 3
RING_ITEMS = [s for s in PASSING if not is_early_lookup(s)]
EARLY_LOOKUPS = [s for s in PASSING if is_early_lookup(s)]


def evacuator(item):
    kind, c, g = item
    if kind == "score":
        return "vector"
    if kind == "onehot" or c == 0:
        return "scalar"
    return "vector" if g % 2 else "scalar"


def evacuations(items):
    return {who: sum(evacuator(x) == who for x in items) for who in ("vector", "scalar")}


def last_user(item):
    line = EARLY_LOOKUPS if item in EARLY_LOOKUPS else RING_ITEMS
    n = line.index(item) - RING
    if n < 0:
        return None
    who = evacuator(line[n])
    return who, evacuations(PASSING[:PASSING.index(line[n]) + 1])[who]


def before(item):
    needed = [x for x in PASSING if x[0] == "onehot" or x[0] == "group" and x[1] <= item[1]]
    if item[1] < LATE_TILE:
        needed = [x for x in needed if x[0] == "group" or is_early_lookup(x)]
    out = {}
    for who in ("vector", "scalar"):
        mine = [x for x in needed if evacuator(x) == who]
        if mine:
            out[who] = evacuations(PASSING[:PASSING.index(mine[-1]) + 1])[who]
    return out


def dlrm_tower(nc, ids_dram, dense_dram, onehot_ids_dram, tables, w1_dram, w2_dram, small_dram, out):
    F32, BF16, F16, I32 = mybir.dt.float32, mybir.dt.bfloat16, mybir.dt.float16, mybir.dt.int32
    ACT = mybir.ActivationFunctionType
    ctx = ExitStack()
    with ctx:
        def sb(name, shape, dt):
            return ctx.enter_context(nc.sbuf_tensor(name, shape, dt))

        def sem(name):
            return ctx.enter_context(nc.semaphore(name))

        nt = len(ONEHOT)
        ids = sb("ids", [P, TILES * F], I32)
        gathered = sb("gathered", [P, TILES, SLOTS - LATE_SLOT, D], F32)
        ident = sb("ident", [P, P], F32)
        row_id = sb("row_id", [P, CHUNKS], F32)
        id_words = sb("id_words", [P, 2, BATCH], I32)
        id_half = sb("id_half", [P, 2, BATCH], F16)
        table = sb("table", [P, TABLE_SLOTS, CHUNKS, D], F32)
        rest = sb("rest", [P, 2, CHUNKS, D], F32)
        low = sb("low", [P, 2, CHUNKS, D], BF16)
        hot = sb("hot", [P, 2, CHUNKS, BATCH], BF16)
        feat = sb("feat", [P, BATCH, WIDTH], F32)
        dense_t = sb("dense_t", [P, BATCH], F32)
        dots = sb("dots", [P, 2, MOVING, QUADS], F32)
        turned = sb("turned", [P, MOVING, WIDTH], F32)
        packed = sb("packed", [P, CHUNKS_OF_PAIRS * P], F32)
        pairs = sb("pairs", [P, 2, CHUNKS_OF_PAIRS, P], F32)
        h1 = sb("h1", [P, H1 // P, BATCH], F32)
        h2 = sb("h2", [P, H2 // P, BATCH], F32)
        w1 = sb("w1", [P, CHUNKS_OF_PAIRS + 2, H1], F32)
        w1_dense = sb("w1_dense", [P, H1], F32)
        w2 = sb("w2", [P, H1 // P, H2], F32)
        small = sb("small", [P, 8], F32)
        y = sb("y", [1, BATCH], F32)

        ring = [ctx.enter_context(nc.psum_tensor(f"ring{i}", [P, 512], F32)) for i in range(RING)]
        dot_banks = [ctx.enter_context(nc.psum_tensor(f"dots{i}", [P, 512], F32)) for i in range(RING)]
        bank_a = ctx.enter_context(nc.psum_tensor("bank_a", [P, 512], F32))
        bank_b = ctx.enter_context(nc.psum_tensor("bank_b", [P, 512], F32))

        ids_in, dense_in, small_in, w1_in, w2_in = (sem(n) for n in (
            "ids_in", "dense_in", "small_in", "w1_in", "w2_in"))
        ident_made, rows_made, ident_zero = sem("ident_made"), sem("rows_made"), sem("ident_zero")
        id_words_in = [sem(f"id_words_in{i}") for i in range(2)]
        id_half_made = sem("id_half_made")
        hot_made = sem("hot_made")
        table_in = [sem(f"table_in{i}") for i in range(TABLE_SLOTS)]
        rest_made, low_made = sem("rest_made"), sem("low_made")
        gather_in = [[sem(f"gather_in{c}_{g}") for g in range(len(GROUPS[c]))] for c in range(TILES)]
        ring_full, lookup_full = sem("ring_full"), sem("lookup_full")
        bank_put = {"vector": sem("bank_put_vector"), "scalar": sem("bank_put_scalar")}
        pads_zero, dense_put = sem("pads_zero"), sem("dense_put")
        dots_full = sem("dots_full")
        dots_put = {"vector": sem("dots_put_vector"), "scalar": sem("dots_put_scalar")}
        turned_made = sem("turned_made")
        packed_put = {"vector": sem("packed_put_vector"), "scalar": sem("packed_put_scalar")}
        w1_dense_made = sem("w1_dense_made")
        STAGES = ("pairs", "hidden1", "hidden2")
        a_full = {s: sem(f"{s}_a_full") for s in STAGES}
        b_full = {s: sem(f"{s}_b_full") for s in STAGES}
        a_put = {s: sem(f"{s}_a_put") for s in STAGES}
        b_put = {s: sem(f"{s}_b_put") for s in STAGES}
        stored = sem("stored")

        block = ctx.enter_context(nc.Block())

        @block.sync
        def _(sp):
            sp.dma_start(ids[:, :], ids_dram).then_inc(ids_in, 16)

            def load_ids(t):
                if t >= 2:
                    sp.wait_ge(id_half_made, t - 1)
                sp.dma_start(id_words[:, t % 2, :],
                             onehot_ids_dram[t:t + 1, :].broadcast_to([P, BATCH])).then_inc(id_words_in[t % 2], 16)

            def load_table(t):
                if t >= TABLE_SLOTS:
                    sp.wait_ge(rest_made, t - TABLE_SLOTS + 1)
                    sp.wait_ge(lookup_full, t - TABLE_SLOTS + 1)
                src = tables[ONEHOT[t]]
                sp.dma_start(table[:, t % TABLE_SLOTS, 0:FULL, :],
                             src[0:FULL * P, :].rearrange("(p n) d -> p n d", n=FULL)).then_inc(table_in[t % TABLE_SLOTS], 16)
                sp.dma_start(table[0:REST, t % TABLE_SLOTS, FULL, :], src[FULL * P:ROWS, :]).then_inc(table_in[t % TABLE_SLOTS], 16)

            load_ids(0)
            load_table(0)
            sp.dma_start(dense_t[:, :], dense_dram).then_inc(dense_in, 16)
            load_ids(1)
            load_table(1)
            load_ids(2)
            load_table(2)
            sp.dma_start(w1[:, :, :], w1_dram).then_inc(w1_in, 16)
            for t in range(3, nt):
                load_ids(t)
                load_table(t)
            sp.dma_start(small[:, :], small_dram).then_inc(small_in, 16)
            sp.dma_start(w2[:, :, :], w2_dram.rearrange("(k p) n -> p k n", p=P)).then_inc(w2_in, 16)
            for who, count in evacuations(PASSING).items():
                sp.wait_ge(bank_put[who], count)
            sp.dma_start(out, y[0:1, :]).then_inc(stored, 16)
            sp.wait_ge(stored, 16)

        @block.gpsimd
        def _(pool):
            nc.gpsimd.memset(ident[:, :], 0.0).then_inc(ident_zero, 1)
            pool.wait_ge(ident_zero, 1)
            nc.gpsimd.affine_select(out=ident[:, :], in_=ident[:, :], compare_op=ALU.not_equal, fill=1.0,
                                    base=0, pattern=[[-1, P]], channel_multiplier=1).then_inc(ident_made, 1)
            nc.gpsimd.iota(row_id[:, 0:FULL], pattern=[[1, FULL]], base=0, channel_multiplier=FULL,
                           allow_small_or_imprecise_dtypes=True).then_inc(rows_made, 1)
            nc.gpsimd.iota(row_id[:, FULL:CHUNKS], pattern=[[1, 1]], base=FULL * P, channel_multiplier=1,
                           allow_small_or_imprecise_dtypes=True).then_inc(rows_made, 1)
            pool.wait_ge(ids_in, 16)
            for c in range(TILES):
                for g, slots in enumerate(GROUPS[c]):
                    for s in slots:
                        f = SLOT_FEATURE[s]
                        nc.gpsimd.indirect_dma_start(
                            out=gathered[:, c, s - LATE_SLOT, :], out_offset=None, in_=tables[f],
                            in_offset=bass.IndirectOffsetOnAxis(ap=ids[:, c * F + f:c * F + f + 1], axis=0),
                        ).then_inc(gather_in[c][g], 16)

        def top_half(words):
            if len(words.shape) == 3:
                return words.bitcast(BF16).rearrange("p n (d half) -> p n d half", half=2)[:, :, :, 1]
            return words.bitcast(BF16).rearrange("p (d half) -> p d half", half=2)[:, :, 1]

        def passing_bank(item):
            if item in EARLY_LOOKUPS:
                n = EARLY_LOOKUPS.index(item)
                return dot_banks[n % RING], lookup_full, n + 1
            n = RING_ITEMS.index(item)
            return ring[n % RING], ring_full, n + 1

        def hidden_banks(c):
            return (bank_a, bank_b) if c < LAST_TILE else (dot_banks[0], dot_banks[1])

        def put_item(engine, copy, item):
            kind, c, g = item
            bank, full, count = passing_bank(item)
            engine.wait_ge(full, count)
            if kind == "score":
                last = copy(y[0:1, c * P:(c + 1) * P], bank[0:1, 0:P])
            elif kind == "onehot":
                cols = lookup_columns(c)
                last = copy(feat[:, cols, 1 + c].rearrange("p (c q k) -> p c k q", q=QUADS, k=QUAD),
                            bank[:, cols].rearrange("p (c k q) -> p c k q", k=QUAD, q=QUADS))
            else:
                s, w = GROUPS[c][g][0], len(GROUPS[c][g])
                last = copy(feat[:, c * P:(c + 1) * P, s:s + w].rearrange("p (q k) s -> p k q s", k=QUAD),
                            bank[:, 0:w * P].rearrange("p (s k q) -> p k q s", s=w, k=QUAD))
            last.then_inc(bank_put[evacuator(item)], 1)

        def put_dots(engine, copy, c, u, quarters, who):
            n = c * UNITS + u
            engine.wait_ge(dots_full, n + 1)
            if c >= 2 and u == 0:
                engine.wait_ge(turned_made, 2 * (c - 1))
            src = dot_banks[n % RING][:, :].rearrange("p (q m) -> p q m", q=UNIT)
            for k in quarters:
                part = slice(WIDTH * k, WIDTH * (k + 1))
                last = copy(dots[part, c % 2, 0:MOVING, UNIT * u:UNIT * (u + 1)],
                            src[part, :, k * MOVING:(k + 1) * MOVING].rearrange("p q m -> p m q"))
            last.then_inc(dots_put[who], 1)

        def pack(engine, copy, c, cuts, who):
            if c:
                engine.wait_ge(b_full["pairs"], c)
            for cut in cuts:
                first, n, width = CUTS[cut]
                cells = packed[:, CUT_CELL[cut]:CUT_CELL[cut + 1]].rearrange("p (j i) -> p j i", i=width)
                copy(cells, turned[:, first:first + n, 0:width]).then_inc(packed_put[who], 1)

        @block.scalar
        def _(act):
            def relu(dst, src, bias):
                return nc.scalar.activation(dst, src, ACT.Relu, bias=bias)

            for item in SCHEDULE:
                kind, c, g = item
                if kind == "prepare":
                    act.wait_ge(id_words_in[c % 2], 16 * (c // 2 + 1))
                    if c >= 2:
                        act.wait_ge(hot_made, CHUNKS * (c - 1))
                    nc.scalar.copy(id_half[:, c % 2, :], id_words[:, c % 2, :]).then_inc(id_half_made, 1)
                elif kind == "dense":
                    act.wait_ge(dense_in, 16)
                    nc.scalar.copy(feat[:, :, 0].rearrange("p (c q k) -> p c k q", q=QUADS, k=QUAD),
                                   dense_t[:, :].rearrange("p (c k q) -> p c k q", k=QUAD, q=QUADS)).then_inc(dense_put, 1)
                elif item in PASSING and evacuator(item) == "scalar":
                    put_item(act, nc.scalar.copy, item)
                elif kind == "dots":
                    put_dots(act, nc.scalar.copy, c, g, (0, 1), "scalar")
                elif kind == "pack":
                    act.wait_ge(turned_made, 2 * c + 1)
                    pack(act, nc.scalar.copy, c, HIGH_CUTS, "scalar")
                elif kind == "pairs":
                    act.wait_ge(a_full["pairs"], c + 1)
                    nc.scalar.copy(pairs[:, c % 2, 2, :], bank_a[:, 0:P]).then_inc(a_put["pairs"], 1)
                elif kind == "hidden1" and g == 0:
                    act.wait_ge(a_full["hidden1"], c + 1)
                    act.wait_ge(small_in, 16)
                    for n in range(2):
                        last = relu(h1[:, n, c * P:(c + 1) * P], hidden_banks(c)[0][:, n * P:(n + 1) * P],
                                    small[:, n:n + 1])
                    last.then_inc(a_put["hidden1"], 1)
                elif kind == "hidden2":
                    act.wait_ge(a_full["hidden2"], c + 1)
                    relu(h2[:, 0, c * P:(c + 1) * P], bank_a[:, 0:P], small[:, 4:5]).then_inc(a_put["hidden2"], 1)
                    if c < LAST_TILE:
                        act.wait_ge(b_full["hidden2"], c + 1)
                        relu(h2[:, 1, c * P:(c + 1) * P], bank_b[:, 0:P], small[:, 5:6]).then_inc(b_put["hidden2"], 1)

        @block.vector
        def _(dve):
            def relu(dst, src, bias):
                return nc.vector.tensor_scalar(dst, src, bias, 0.0, ALU.add, ALU.max)

            nc.vector.memset(feat[:, :, SLOTS:WIDTH], 0.0).then_inc(pads_zero, 1)
            for item in SCHEDULE:
                kind, c, g = item
                if kind == "prepare":
                    dve.wait_ge(id_half_made, c + 1)
                    if c == 0:
                        dve.wait_ge(rows_made, 2)
                    if c >= 2:
                        dve.wait_ge(lookup_full, c - 1)
                    cols = lookup_columns(c)
                    for n in range(CHUNKS):
                        k = P if n < FULL else REST
                        nc.vector.tensor_scalar(hot[0:k, c % 2, n, cols], id_half[0:k, c % 2, cols],
                                                row_id[0:k, n:n + 1], None, ALU.is_equal).then_inc(hot_made, 1)
                    dve.wait_ge(table_in[c % TABLE_SLOTS], 32 * (c // TABLE_SLOTS + 1))
                    for n, k in SPANS:
                        last = nc.vector.tensor_tensor(rest[0:k, c % 2, n, :], table[0:k, c % TABLE_SLOTS, n, :],
                                                       top_half(table[0:k, c % TABLE_SLOTS, n, :]), ALU.subtract)
                    last.then_inc(rest_made, 1)
                    dve.wait_ge(rest_made, c + 1)
                    for n, k in SPANS:
                        last = nc.vector.tensor_tensor(low[0:k, c % 2, n, :], rest[0:k, c % 2, n, :],
                                                       top_half(rest[0:k, c % 2, n, :]), ALU.subtract)
                    last.then_inc(low_made, 1)
                elif item in PASSING and evacuator(item) == "vector":
                    put_item(dve, nc.vector.tensor_copy, item)
                elif kind == "dots":
                    put_dots(dve, nc.vector.tensor_copy, c, g, (2, 3), "vector")
                elif kind == "fold":
                    dve.wait_ge(w1_in, 16)
                    nc.vector.tensor_tensor(w1_dense[:, :], w1[:, CHUNKS_OF_PAIRS, :], w1[:, CHUNKS_OF_PAIRS + 1, :],
                                            ALU.add).then_inc(w1_dense_made, 1)
                elif kind == "pack":
                    dve.wait_ge(dots_put["scalar"], (c + 1) * UNITS)
                    dve.wait_ge(dots_put["vector"], (c + 1) * UNITS)
                    if c:
                        dve.wait_ge(packed_put["scalar"], c * len(HIGH_CUTS))
                        dve.wait_ge(packed_put["vector"], c * len(LOW_CUTS))
                    for part in (slice(HIGH, MOVING), slice(0, HIGH)):
                        nc.vector.transpose(turned[:, part, :], dots[:, c % 2, part, :]).then_inc(turned_made, 1)
                    dve.wait_ge(turned_made, 2 * c + 2)
                    pack(dve, nc.vector.tensor_copy, c, LOW_CUTS, "vector")
                elif kind == "pairs":
                    dve.wait_ge(b_full["pairs"], c + 1)
                    nc.vector.tensor_copy(pairs[:, c % 2, 0:2, :],
                                          bank_b[:, 0:2 * P].rearrange("p (n b) -> p n b", n=2)).then_inc(b_put["pairs"], 1)
                elif kind == "hidden1" and g == 1:
                    dve.wait_ge(b_full["hidden1"], c + 1)
                    dve.wait_ge(small_in, 16)
                    for n in range(2):
                        last = relu(h1[:, 2 + n, c * P:(c + 1) * P], hidden_banks(c)[1][:, n * P:(n + 1) * P],
                                    small[:, 2 + n:3 + n])
                    last.then_inc(b_put["hidden1"], 1)
                elif kind == "hidden2" and c == LAST_TILE:
                    dve.wait_ge(b_full["hidden2"], c + 1)
                    dve.wait_ge(b_put["hidden2"], c)
                    relu(h2[:, 1, c * P:(c + 1) * P], bank_b[:, 0:P], small[:, 5:6]).then_inc(b_put["hidden2"], 1)

        @block.tensor
        def _(pe):
            def first_layer(c, n, dense_part, pairs_part):
                dst = hidden_banks(c)[n // 2][:, (n % 2) * P:(n % 2 + 1) * P]
                ns = slice(n * P, (n + 1) * P)
                if dense_part:
                    last = nc.tensor.matmul(dst, w1_dense[:, ns], dense_t[:, c * P:(c + 1) * P],
                                            start=pairs_part or n % 2 == 0, stop=False, skip_group_check=True)
                if pairs_part:
                    for chunk in range(CHUNKS_OF_PAIRS):
                        last = nc.tensor.matmul(dst, w1[:, chunk, ns], pairs[:, c % 2, chunk, :], start=False,
                                                stop=(chunk == CHUNKS_OF_PAIRS - 1), skip_group_check=True)
                return last

            pe.wait_ge(ident_made, 1)
            for _ in range(WARM_UP):
                nc.tensor.matmul(bank_a[:, 0:P], ident[:, :], ident[:, :], start=True, stop=True)
            for item in SCHEDULE:
                kind, c, g = item
                cols = slice(c * P, (c + 1) * P)
                if item in PASSING:
                    bank, full, _ = passing_bank(item)
                    free = last_user(item)
                    if free:
                        pe.wait_ge(bank_put[free[0]], free[1])
                if kind == "onehot":
                    pe.wait_ge(table_in[c % TABLE_SLOTS], 32 * (c // TABLE_SLOTS + 1))
                    cols = lookup_columns(c)
                    for part in range(PARTS):
                        if part == 1:
                            pe.wait_ge(rest_made, c + 1)
                        if part == 2:
                            pe.wait_ge(low_made, c + 1)
                        for n in range(CHUNKS):
                            k = P if n < FULL else REST
                            if part == 0:
                                pe.wait_ge(hot_made, CHUNKS * c + n + 1)
                                weights = top_half(table[0:k, c % TABLE_SLOTS, n, :])
                            elif part == 1:
                                weights = top_half(rest[0:k, c % 2, n, :])
                            else:
                                weights = low[0:k, c % 2, n, :]
                            last = nc.tensor.matmul(bank[:, cols], weights, hot[0:k, c % 2, n, cols],
                                                    start=(part == 0 and n == 0),
                                                    stop=(part == PARTS - 1 and n == CHUNKS - 1))
                    last.then_inc(full, 1)
                elif kind == "group":
                    pe.wait_ge(gather_in[c][g], 16 * len(GROUPS[c][g]))
                    for n, s in enumerate(GROUPS[c][g]):
                        last = nc.tensor.transpose(bank[:, n * P:(n + 1) * P], gathered[:, c, s - LATE_SLOT, :],
                                                   ident[:, :])
                    last.then_inc(full, 1)
                elif kind == "dots":
                    n = c * UNITS + g
                    if g == 0:
                        for who, count in before(item).items():
                            if count:
                                pe.wait_ge(bank_put[who], count)
                        if c == 0:
                            pe.wait_ge(pads_zero, 1)
                            pe.wait_ge(dense_put, 1)
                    if n >= RING:
                        pe.wait_ge(dots_put["scalar"], n - RING + 1)
                        pe.wait_ge(dots_put["vector"], n - RING + 1)
                    for q in range(UNIT):
                        b = c * P + (g * UNIT + q) * QUAD
                        still = feat[:, b:b + QUAD, :].rearrange("p b s -> p (b s)")
                        last = nc.tensor.matmul(dot_banks[n % RING][:, q * P:q * P + QUAD * MOVING], still,
                                                feat[:, b:b + QUAD, 1:SLOTS], start=True, stop=True)
                    last.then_inc(dots_full, 1)
                elif kind == "pairs":
                    if c:
                        pe.wait_ge(a_put["hidden2"], c)
                        pe.wait_ge(b_put["hidden2"], c)
                    pe.wait_ge(packed_put["scalar"], len(HIGH_CUTS) * (c + 1))
                    nc.tensor.transpose(bank_a[:, 0:P], packed[:, 2 * P:3 * P], ident[:, :]).then_inc(a_full["pairs"], 1)
                    nc.tensor.transpose(bank_b[:, P:2 * P], packed[:, P:2 * P], ident[:, :])
                    pe.wait_ge(packed_put["vector"], len(LOW_CUTS) * (c + 1))
                    nc.tensor.transpose(bank_b[:, 0:P], packed[:, 0:P], ident[:, :]).then_inc(b_full["pairs"], 1)
                elif kind == "hidden1_dense":
                    pe.wait_ge(dots_put["scalar"], TILES * UNITS)
                    pe.wait_ge(dots_put["vector"], TILES * UNITS)
                    for n in range(H1 // P):
                        first_layer(c, n, True, False)
                elif kind == "hidden1":
                    if c == 0:
                        pe.wait_ge(w1_dense_made, 1)
                    pe.wait_ge(a_put["pairs"], c + 1)
                    pe.wait_ge(b_put["pairs"], c + 1)
                    for n in (2 * g, 2 * g + 1):
                        last = first_layer(c, n, c < LAST_TILE, True)
                    last.then_inc((a_full, b_full)[g]["hidden1"], 1)
                elif kind == "hidden2":
                    if c == 0:
                        pe.wait_ge(w2_in, 16)
                    pe.wait_ge(a_put["hidden1"], c + 1)
                    if c < LAST_TILE:
                        pe.wait_ge(b_put["hidden1"], c + 1)
                    for half in range(2):
                        if half:
                            pe.wait_ge(b_put["hidden1"], c + 1)
                        for m, bank in enumerate((bank_a, bank_b)):
                            for n in (2 * half, 2 * half + 1):
                                last = nc.tensor.matmul(bank[:, 0:P], w2[:, n, m * P:(m + 1) * P], h1[:, n, cols],
                                                        start=(n == 0), stop=(n == H1 // P - 1))
                            if half:
                                last.then_inc((a_full, b_full)[m]["hidden2"], 1)
                elif kind == "score":
                    pe.wait_ge(a_put["hidden2"], c + 1)
                    pe.wait_ge(b_put["hidden2"], c + 1)
                    for m in range(H2 // P):
                        last = nc.tensor.matmul(bank[0:1, 0:P], small[:, 6 + m:7 + m], h2[:, m, cols],
                                                start=(m == 0), stop=(m == H2 // P - 1))
                    last.then_inc(full, 1)


def kernel(**inputs):
    import numpy as np
    import concourse.bacc as bacc
    from concourse.bass_utils import run_bass_kernel_spmd as run

    x = {name: np.asarray(a) for name, a in inputs.items()}
    w1 = x["W_top1"]
    w1_tiles = np.zeros((P, CHUNKS_OF_PAIRS + 2, H1), w1.dtype)
    for cell, row in pair_row_places():
        w1_tiles[cell % P, cell // P] = w1[row]
    w1_tiles[:, CHUNKS_OF_PAIRS] = w1[0:D]
    w1_tiles[:, CHUNKS_OF_PAIRS + 1] = w1[w1.shape[0] - D:]
    small = np.concatenate([x["b_top1"].reshape(-1, P).T, x["b_top2"].reshape(-1, P).T,
                            x["W_top3"].reshape(-1, P).T], axis=1)
    arrays = {
        "ids": x["ids"].reshape(TILES, P, F).transpose(1, 0, 2).reshape(P, TILES * F),
        "dense": x["r_dense_features"].T,
        "onehot_ids": x["ids"].T[ONEHOT],
        "w1": w1_tiles, "w2": x["W_top2"], "small": small,
    }
    arrays.update({f"tbl_{f}": x[f"tbl_{f}"] for f in range(F)})
    arrays = {name: np.ascontiguousarray(a) for name, a in arrays.items()}

    nc = bacc.Bacc("TRN2", target_bir_lowering=False, num_devices=1)
    ap = {name: nc.dram_tensor("in_" + name, a.shape, mybir.dt.from_np(a.dtype), kind="ExternalInput").ap()
          for name, a in arrays.items()}
    out = nc.dram_tensor("scores", (BATCH, 1), mybir.dt.float32, kind="ExternalOutput").ap()
    dlrm_tower(nc, ap["ids"], ap["dense"], ap["onehot_ids"], [ap[f"tbl_{f}"] for f in range(F)],
               ap["w1"], ap["w2"], ap["small"], out.rearrange("b o -> o b"))
    result = run(nc, [{"in_" + name: a for name, a in arrays.items()}], core_ids=[0])
    return result.results[0]["scores"]
```
